# Optimizing a Trainium2 kernel written in Bass

```python
import numpy as np
import jax
import jax.numpy as jnp

def _softmax(x, axis=-1):
    return jax.nn.softmax(x, axis=axis)

def _gelu(x):
    return jax.nn.gelu(x, approximate=True)

def _silu(x):
    return jax.nn.silu(x)

def _sigmoid(x):
    return jax.nn.sigmoid(x)

def _layernorm(x, axis=-1, eps=1e-05):
    m = jnp.mean(x, axis=axis, keepdims=True)
    v = jnp.var(x, axis=axis, keepdims=True)
    return (x - m) / jnp.sqrt(v + eps)

def _scatter_add(tgt, idx, src, axis=0):
    return tgt.at[idx].add(src)

def _segment_sum(src, seg, n):
    return jax.ops.segment_sum(src, seg, n)
kernel_name = 'mk_recurrent_d1_jaxref_r4_bf5041'

def setup_inputs(seed: int=0):
    np.random.seed(seed)
    _w = jnp.asarray

    def _L0_attn_setup():
        import jax, jax.numpy as jnp
        import numpy as np
        D_MODEL = 256
        H = 4
        DK = 128
        DV = 64
        EPS = 1e-05
        SCALE = DK ** (-0.5)

        def _delta_rule(q, k, v, beta):
            b = q.shape[0]
            qt = jnp.moveaxis(q, 1, 0)
            kt = jnp.moveaxis(k, 1, 0)
            vt = jnp.moveaxis(v, 1, 0)
            bt = jnp.moveaxis(beta, 1, 0)
            S0 = jnp.zeros((b, H, DK, DV), q.dtype)

            def step(S, inp):
                q_t, k_t, v_t, b_t = inp
                pred = jnp.einsum('bhk,bhkv->bhv', k_t, S)
                delta = (v_t - pred) * b_t[..., None]
                S = S + k_t[..., :, None] * delta[..., None, :]
                o_t = jnp.einsum('bhk,bhkv->bhv', q_t, S)
                return (S, o_t)
            _, o = jax.lax.scan(step, S0, (qt, kt, vt, bt))
            return jnp.moveaxis(o, 0, 1)
        key = jax.random.key(seed)
        ks = jax.random.split(key, 8)
        w = lambda k, i, o: jax.random.normal(k, (i, o), jnp.float32) * 2.0 ** (-2.5) * (6.0 / (i + o)) ** 0.5 * 2
        return {'x': jax.random.normal(ks[0], (2, 1024, D_MODEL), jnp.float32), 'Wq': w(ks[1], D_MODEL, H * DK), 'Wk': w(ks[2], D_MODEL, H * DK), 'Wv': w(ks[3], D_MODEL, H * DV), 'Wb': w(ks[4], D_MODEL, H), 'Wg': w(ks[5], D_MODEL, H * DV), 'Wo': w(ks[6], H * DV, D_MODEL), 'norm_w': jnp.ones((DV,), jnp.float32)}
    _L0_attn_in = _L0_attn_setup()

    def _L0_ffn_setup():
        import jax, jax.numpy as jnp
        import numpy as np
        B, T, D, E = (4, 256, 256, 8)
        HD = 4 * D
        key = jax.random.key(seed)
        k1, k2, k3, k4 = jax.random.split(key, 4)
        std = 0.5 * D ** (-0.5)
        bound = 3.0 ** 0.5 * std
        x = jax.random.normal(k1, (B, T, D), dtype=jnp.float32)
        router_w = jax.random.normal(k2, (E, D), dtype=jnp.float32) * 0.02
        expert_fc = jax.random.uniform(k3, (E, D, HD), dtype=jnp.float32, minval=-bound, maxval=bound)
        expert_proj = jax.random.normal(k4, (E, D, HD), dtype=jnp.float32) * 0.02
        return {'x': x, 'router_w': router_w, 'expert_fc': expert_fc, 'expert_proj': expert_proj}
    _L0_ffn_in = _L0_ffn_setup()
    _d = {'L0_attn_x': _L0_attn_in['x'], 'L0_attn_Wq': _L0_attn_in['Wq'], 'L0_attn_Wk': _L0_attn_in['Wk'], 'L0_attn_Wv': _L0_attn_in['Wv'], 'L0_attn_Wb': _L0_attn_in['Wb'], 'L0_attn_Wg': _L0_attn_in['Wg'], 'L0_attn_Wo': _L0_attn_in['Wo'], 'L0_attn_norm_w': _L0_attn_in['norm_w'], 'L0_ffn_router_w': _L0_ffn_in['router_w'], 'L0_ffn_expert_fc': _L0_ffn_in['expert_fc'], 'L0_ffn_expert_proj': _L0_ffn_in['expert_proj']}
    _x0 = _d['L0_attn_x']
    _d['L0_attn_x'] = jax.random.normal(jax.random.fold_in(jax.random.key(seed), 1), (2, 2048, 256), dtype=_x0.dtype)
    del _x0
    return _d

def reference(L0_attn_x, L0_attn_Wq, L0_attn_Wk, L0_attn_Wv, L0_attn_Wb, L0_attn_Wg, L0_attn_Wo, L0_attn_norm_w, L0_ffn_router_w, L0_ffn_expert_fc, L0_ffn_expert_proj):

    def _L0_attn_ref(x, Wq, Wk, Wv, Wb, Wg, Wo, norm_w):
        import jax, jax.numpy as jnp
        import numpy as np
        D_MODEL = 256
        H = 4
        DK = 128
        DV = 64
        EPS = 1e-05
        SCALE = DK ** (-0.5)

        def _delta_rule(q, k, v, beta):
            b = q.shape[0]
            qt = jnp.moveaxis(q, 1, 0)
            kt = jnp.moveaxis(k, 1, 0)
            vt = jnp.moveaxis(v, 1, 0)
            bt = jnp.moveaxis(beta, 1, 0)
            S0 = jnp.zeros((b, H, DK, DV), q.dtype)

            def step(S, inp):
                q_t, k_t, v_t, b_t = inp
                pred = jnp.einsum('bhk,bhkv->bhv', k_t, S)
                delta = (v_t - pred) * b_t[..., None]
                S = S + k_t[..., :, None] * delta[..., None, :]
                o_t = jnp.einsum('bhk,bhkv->bhv', q_t, S)
                return (S, o_t)
            _, o = jax.lax.scan(step, S0, (qt, kt, vt, bt))
            return jnp.moveaxis(o, 0, 1)
        b, n, _ = x.shape
        q = (x @ Wq).reshape(b, n, H, DK)
        k = (x @ Wk).reshape(b, n, H, DK)
        v = (x @ Wv).reshape(b, n, H, DV)
        beta = jax.nn.sigmoid(x @ Wb)
        k = k * jax.lax.rsqrt(jnp.sum(k * k, axis=-1, keepdims=True) + 1e-12)
        q = q * SCALE
        o = _delta_rule(q, k, v, beta)
        g = (x @ Wg).reshape(b, n, H, DV)
        o = o * jax.lax.rsqrt(jnp.mean(o * o, axis=-1, keepdims=True) + EPS) * norm_w
        o = o * (g * jax.nn.sigmoid(g))
        return o.reshape(b, n, H * DV) @ Wo

    def _L0_ffn_ref(x, router_w, expert_fc, expert_proj):
        import jax, jax.numpy as jnp
        import numpy as np
        B, T, D, E = (4, 256, 256, 8)
        HD = 4 * D
        logits = jnp.einsum('btd,ed->bte', x, router_w)
        probs = jax.nn.softmax(logits, axis=-1)
        expert_ids = jnp.argmax(probs, axis=-1)
        mask = jax.nn.one_hot(expert_ids, E, dtype=x.dtype)
        h = jnp.einsum('btd,edh->ebth', x, expert_fc)
        h = jnp.square(jax.nn.relu(h))
        out_e = jnp.einsum('ebth,edh->ebtd', h, expert_proj)
        output = jnp.einsum('ebtd,bte->btd', out_e, mask)
        return output
    x = L0_attn_x
    xn = _layernorm(x, axis=-1)
    s = _L0_attn_ref(xn, L0_attn_Wq, L0_attn_Wk, L0_attn_Wv, L0_attn_Wb, L0_attn_Wg, L0_attn_Wo, L0_attn_norm_w)
    g = _silu(_L0_ffn_ref(xn, L0_ffn_router_w, L0_ffn_expert_fc, L0_ffn_expert_proj))
    x = x + s * g
    return x

_drawn_inputs = setup_inputs


def setup_inputs(seed=0):
    import zlib

    import numpy as np

    out = dict(_drawn_inputs(seed))
    spreads = {'L0_attn_norm_w': (1.0, 0.6)}
    factors = {'L0_attn_Wq': 2.696,
     'L0_attn_Wk': 2.7,
     'L0_attn_Wv': 2.707,
     'L0_attn_Wb': 8.0,
     'L0_attn_Wg': 2.802,
     'L0_attn_Wo': 2.697,
     'L0_ffn_router_w': 2.906,
     'L0_ffn_expert_fc': 2.989,
     'L0_ffn_expert_proj': 2.72}
    for name, (base, spread) in spreads.items():
        noise = np.random.default_rng([zlib.crc32(name.encode()), seed]).standard_normal(out[name].shape)
        drawn = base * np.exp(spread * noise) if base else spread * noise
        out[name] = jnp.asarray(drawn.astype(out[name].dtype))
    for name, factor in factors.items():
        out[name] = (out[name] * factor).astype(out[name].dtype)
    return out
```

```python
from contextlib import ExitStack

import concourse.bass as bass
from concourse import mybir
from concourse.alu_op_type import AluOpType as ALU

ACT = mybir.ActivationFunctionType
AX_X = mybir.AxisListType.X
F32 = mybir.dt.float32
F16 = mybir.dt.float16
I32 = mybir.dt.int32
U32 = mybir.dt.uint32

P = 128
B, N, D = 2, 2048, 256
H, DK, DV = 4, 128, 64
E, HD = 8, 1024
KC = D // P
NCH = N // P
NQ = B * NCH
NS = B * H
HC = HD // P
NT = NQ + E - 1
LEVELS = [1, 2, 4, 8, 16, 32, 64]
SCALE = DK ** -0.5
LN_EPS, RMS_EPS, K_EPS = 1e-5, 1e-5, 1e-12


class Signal:

    def __init__(self, sem, ahead=0):
        self.sem, self.ahead = sem, ahead


class Step:

    def __init__(self, eng, number):
        self.eng = eng
        self.plus1 = eng.snap(number + 1)
        self.plus2 = eng.snap(number + 2)

    def this(self, *signals):
        for s in signals:
            self.eng.wait_ge(s.sem, self.plus2 if s.ahead else self.plus1)

    def last(self, *signals):
        for s in signals:
            assert s.ahead
            self.eng.wait_ge(s.sem, self.plus1)


class Levels:

    def __init__(self, eng, number):
        n = len(LEVELS)
        self.eng = eng
        self.values = [eng.snap(number * n + l + 1) for l in range(n)]

    def at(self, l, *sems):
        for s in sems:
            self.eng.wait_ge(s, self.values[l])


def build_program(nc, x, wq, wk, wvg, wbr, wo, norm_w, fc, pj, out):
    with ExitStack() as ctx:
        def sb(name, shape, dt=F32):
            return ctx.enter_context(nc.sbuf_tensor(name, shape, dt))

        def sem(name):
            return ctx.enter_context(nc.semaphore(name))

        def signal(name, ahead=0):
            return Signal(sem(name), ahead)

        def scratch(name, shape, dt=F32):
            return nc.dram_tensor(name, shape, dt, kind="Internal").ap()

        xnT_d = scratch("xnT_d", [NQ, P, KC * P])
        sorted_x_d = scratch("sorted_x_d", [NT * P, D])
        sorted_y_d = scratch("sorted_y_d", [NT * P, D])
        s_d = scratch("s_d", [NQ, P, D])

        fc_sb = sb("fc_sb", [P, E, KC, HD])
        pj_sb = sb("pj_sb", [P, E, HC, D])
        x_all = pj_sb[:, E // 2:, :, :].rearrange("p e c d -> p (e c) d")
        wq_sb = sb("wq_sb", [P, KC, H * DK])
        wk_sb = sb("wk_sb", [P, KC, H * DK])
        wvg_sb = sb("wvg_sb", [P, KC, 2 * H * DV])
        wbr_sb = sb("wbr_sb", [P, KC, H + E])
        wo_sb = sb("wo_sb", [P, KC, D])
        nw_sb = sb("nw_sb", [P, 1])
        ident = sb("ident", [P, P])
        ident16 = sb("ident16", [P, P], F16)
        negid16 = sb("negid16", [P, P], F16)
        up_neg = sb("up_neg", [P, P])
        up_incl = sb("up_incl", [P, P])
        up_incl16 = sb("up_incl16", [P, P], F16)
        ones16 = sb("ones16", [P, P], F16)
        lvl_mask = sb("lvl_mask", [P, len(LEVELS), P // 2], F16)
        halves = sb("halves", [P, NQ])
        k_eps = sb("k_eps", [P, NS])
        o_eps = sb("o_eps", [P, NS])
        pm1 = sb("pm1", [P, NS, P], F16)
        logits = sb("logits", [P, NQ, H + E])
        beta = sb("beta", [P, NQ, H])
        mean = sb("mean", [P, NQ])
        rstd = sb("rstd", [P, NQ])
        pos = sb("pos", [P, NQ], I32)
        tile_e = sb("tile_e", [1, NT], I32)

        psum = [ctx.enter_context(nc.psum_tensor(f"bank{i}", [P, 512], F32)) for i in range(8)]

        work = ExitStack()
        with work:
            def tmp(name, shape, dt=F32):
                return work.enter_context(nc.sbuf_tensor(name, shape, dt))

            stats = tmp("stats", [P, NQ, 6])
            dmean = tmp("dmean", [P, NQ])
            zeros = tmp("zeros", [P, 3 * D])
            xn_t = [tmp(f"xn_t{b}", [P, KC, P]) for b in range(B)]
            xnT_t = [tmp(f"xnT_t{b}", [P, KC, P]) for b in range(B)]
            top = tmp("top", [P, NQ])
            onehot = tmp("onehot", [P, NQ, E])
            onehot16 = tmp("onehot16", [P, NQ, E], F16)
            first = tmp("first", [P, NQ, E])
            prefer = tmp("prefer", [P, E])
            cum = [tmp(f"cum{k}", [P, NQ, E]) for k in range(2)]
            row = tmp("row", [P, NQ, E])
            count_i = tmp("count_i", [P, E], I32)
            padded = tmp("padded", [P, E])
            ends = tmp("ends", [P, E + 1])
            tile_row = tmp("tile_row", [1, NT])
            tile_ef = tmp("tile_ef", [1, NT])
            posf = tmp("posf", [P, NQ])

            x_in = [sem(f"x_in{k}") for k in range(NCH // 4)]
            w_in, experts_in = sem("w_in"), sem("experts_in")
            consts = sem("consts")
            zeroed = sem("zeroed")
            zero_rows = sem("zero_rows")
            stat = sem("stat")
            stat_tmp = sem("stat_tmp")
            rstd_done = sem("rstd_done")
            xn_done = [signal(f"xn_done{b}") for b in range(B)]
            xn_inplace = sem("xn_inplace")
            xnT_ps = [signal(f"xnT_ps{b}") for b in range(B)]
            xnT_sb = [signal(f"xnT_sb{b}", 1) for b in range(B)]
            xnT_out = [sem(f"xnT_out{b}") for b in range(B)]
            lg_ps = [signal(f"lg_ps{b}", 1) for b in range(B)]
            lg_sb = [signal(f"lg_sb{b}", 1) for b in range(B)]
            route = sem("route")
            route_pe = sem("route_pe")
            onehot_done = sem("onehot_done")
            beta_done = sem("beta_done")
            pos_done = sem("pos_done")
            scattered = sem("scattered")

            x_v = x.rearrange("b (c p) d -> b p c d", p=P)
            with nc.Block() as block:
                @block.sync
                def _(sp):
                    xa = x_all.rearrange("p (c b) d -> p b c d", b=B)
                    for c in range(0, NCH, 4):
                        for b in range(B):
                            sp.dma_start(xa[:, b, c:c + 4, :], x_v[b, :, c:c + 4, :]).then_inc(x_in[c // 4], 16)
                    sp.dma_start(wbr_sb[:], wbr.rearrange("(k p) n -> p k n", p=P)).then_inc(w_in, 16)
                    sp.dma_start(wq_sb[:], wq.rearrange("(k p) n -> p k n", p=P)).then_inc(w_in, 16)
                    sp.dma_start(wk_sb[:], wk.rearrange("(k p) n -> p k n", p=P)).then_inc(w_in, 16)
                    sp.dma_start(wvg_sb[:], wvg.rearrange("(k p) n -> p k n", p=P)).then_inc(w_in, 16)
                    sp.dma_start(wo_sb[:], wo.rearrange("(k p) n -> p k n", p=P)).then_inc(w_in, 16)
                    sp.dma_start(nw_sb[:], norm_w).then_inc(w_in, 16)
                    sp.wait_ge(zeroed, 1)
                    with sp.Fori(0, NT // 3) as j:
                        sp.dma_start(
                            sorted_x_d.rearrange("(j p r) d -> j p (r d)", p=P, r=3)[bass.ds(j, 1)].rearrange("a p n -> (a p) n"),
                            zeros[:]).then_inc(zero_rows, 16)
                    for e in range(E):
                        sp.dma_start(fc_sb[:, e], fc[e].rearrange("(k p) n -> p k n", p=P)).then_inc(experts_in, 16)
                    for e in range(E // 2):
                        sp.dma_start(pj_sb[:, e], pj[e].rearrange("(c p) n -> p c n", p=P)).then_inc(experts_in, 16)
                    with sp.Fori(0, NCH) as i:
                        st = Step(sp, i)
                        for b in range(B):
                            st.this(xnT_sb[b])
                            sp.dma_start(xnT_d[bass.ds(2 * i + b, 1)].rearrange("a p n -> p (a n)"),
                                         xnT_t[b][:].rearrange("p k n -> p (k n)")).then_inc(xnT_out[b], 16)
                    for b in range(B):
                        sp.wait_ge(xnT_out[b], 16 * (NCH + 1))
                    sp.wait_ge(scattered, 16 * NQ)
                    for e in range(E // 2, E):
                        sp.dma_start(pj_sb[:, e], pj[e].rearrange("(c p) n -> p c n", p=P)).then_inc(experts_in, 16)
                    sp.wait_ge(experts_in, 16 * 2 * E)

                @block.gpsimd
                def _(pool):
                    pool.memset(zeros[:], 0.0).then_inc(zeroed, 1)
                    n = 0

                    def c(ins):
                        nonlocal n
                        n += 1
                        ins.then_inc(consts, 1)
                        pool.wait_ge(consts, n)

                    def select(t, base, cm, pattern, op, fill=0.0):
                        c(pool.affine_select(out=t, in_=t, compare_op=op, fill=fill, base=base,
                                             pattern=pattern, channel_multiplier=cm))

                    c(pool.memset(halves[:], -0.5))
                    c(pool.memset(k_eps[:], K_EPS))
                    c(pool.memset(o_eps[:], RMS_EPS / SCALE ** 2))
                    c(pool.memset(ident[:], 0.0))
                    select(ident[:], 0, 1, [[-1, P]], ALU.not_equal, 1.0)
                    c(pool.tensor_copy(ident16[:], ident[:]))
                    c(pool.memset(negid16[:], 0.0))
                    select(negid16[:], 0, 1, [[-1, P]], ALU.not_equal, -1.0)
                    c(pool.memset(up_neg[:], -1.0))
                    select(up_neg[:], 0, -1, [[1, P]], ALU.is_gt)
                    c(pool.memset(up_incl[:], 1.0))
                    select(up_incl[:], 0, -1, [[1, P]], ALU.is_ge)
                    c(pool.tensor_copy(up_incl16[:], up_incl[:]))
                    c(pool.memset(ones16[:], 1.0))
                    c(pool.memset(lvl_mask[:], 1.0))
                    for k, s in enumerate(LEVELS):
                        m = lvl_mask[:, k, :].rearrange("p (n c) -> p n c", c=s)
                        select(m, -s, 1, [[-2 * s, P // 2 // s], [0, s]], ALU.is_ge)
                        select(m, 2 * s - 1, -1, [[2 * s, P // 2 // s], [0, s]], ALU.is_ge)
                    for h in range(NS):
                        c(pool.tensor_copy(pm1[:, h, :], ident16[:]))
                    c(pool.iota(tile_row[:], [[P, NT]], base=0, channel_multiplier=0,
                                allow_small_or_imprecise_dtypes=True))
                    c(pool.iota(prefer[:], [[-1, E]], base=E, channel_multiplier=0,
                                allow_small_or_imprecise_dtypes=True))
                    pool.wait_ge(stat, 7)
                    pool.tensor_tensor(rstd[:], rstd[:], halves[:], ALU.pow).then_inc(rstd_done, 1)
                    pool.wait_ge(xn_inplace, 1)
                    pool.wait_ge(zero_rows, 16 * (NT // 3))
                    pool.wait_ge(pos_done, 1)
                    for q in range(NQ):
                        pool.indirect_dma_start(
                            out=sorted_x_d, out_offset=bass.IndirectOffsetOnAxis(ap=pos[:, q:q + 1].bitcast(U32), axis=0),
                            in_=x_all[:, q, :], in_offset=None).then_inc(scattered, 16)
                    pool.wait_ge(scattered, 16 * NQ)

                n_consts = 15 + 2 * len(LEVELS) + NS + 2

                @block.vector
                def _(dve):
                    for b in range(B):
                        dve.sem_inc(lg_sb[b].sem, 1)
                    for q in range(0, NQ, 8):
                        dve.wait_ge(x_in[q // 8], 16 * B)
                        with dve.Fori(q, q + 8) as t:
                            dve.bn_stats(stats[:, bass.ds(t, 1), :].rearrange("p a d -> p (a d)"),
                                         x_all[:, bass.ds(t, 1), :].rearrange("p a d -> p (a d)")).then_inc(stat_tmp, 1)
                    dve.wait_ge(stat_tmp, NQ)
                    me, se, mo, so = (stats[:, :, k] for k in (1, 2, 4, 5))

                    def chained(n, ins):
                        ins.then_inc(stat, 1)
                        dve.wait_ge(stat, n)

                    chained(1, dve.tensor_tensor(mean[:], me, mo, ALU.add))
                    chained(2, dve.tensor_scalar(mean[:], mean[:], 0.5, None, ALU.mult))
                    chained(3, dve.tensor_tensor(dmean[:], mean[:], me, ALU.subtract))
                    chained(4, dve.tensor_tensor(dmean[:], dmean[:], dmean[:], ALU.mult))
                    chained(5, dve.tensor_tensor(rstd[:], se, so, ALU.add))
                    chained(6, dve.tensor_scalar(rstd[:], rstd[:], 1.0 / D, LN_EPS, ALU.mult, ALU.add))
                    chained(7, dve.tensor_tensor(rstd[:], rstd[:], dmean[:], ALU.add))
                    dve.wait_ge(rstd_done, 1)
                    with dve.Fori(0, NCH) as i:
                        st = Step(dve, i)
                        for b in range(B):
                            t = 2 * i + b
                            xt = x_all[:, bass.ds(t, 1), :].rearrange("p a d -> p (a d)")
                            mu, rs = mean[:, bass.ds(t, 1)], rstd[:, bass.ds(t, 1)]
                            st.last(xnT_sb[b])
                            dve.tensor_scalar(xn_t[b][:].rearrange("p k n -> p (k n)"), xt, mu, rs,
                                              ALU.subtract, ALU.mult).then_inc(xn_done[b].sem, 1)
                            dve.tensor_scalar(xt, xt, mu, rs, ALU.subtract, ALU.mult)
                        for b in range(B):
                            t = 2 * i + b
                            st.this(lg_ps[b])
                            dve.tensor_copy(logits[:, bass.ds(t, 1), :].rearrange("p a d -> p (a d)"),
                                            psum[2 + b][:, 0:H + E]).then_inc(lg_sb[b].sem, 1)
                    k = 0

                    def r(ins):
                        nonlocal k
                        k += 1
                        ins.then_inc(route, 1)
                        dve.wait_ge(route, k)

                    for b in range(B):
                        dve.wait_ge(lg_sb[b].sem, NCH + 1)
                    dve.wait_ge(consts, n_consts)
                    lg = logits[:, :, H:]
                    wide = [P, NQ, E]
                    r(dve.tensor_reduce(top[:], lg, AX_X, ALU.max))
                    r(dve.tensor_tensor(first[:], lg, top[:].unsqueeze(2).to_broadcast(wide), ALU.is_ge))
                    r(dve.tensor_tensor(first[:], first[:], prefer[:].unsqueeze(1).to_broadcast(wide), ALU.mult))
                    r(dve.tensor_reduce(top[:], first[:], AX_X, ALU.max))
                    r(dve.tensor_tensor(onehot[:], first[:], top[:].unsqueeze(2).to_broadcast(wide), ALU.is_equal))
                    r(dve.tensor_copy(onehot16[:], onehot[:]))
                    dve.sem_inc(onehot_done, 1)
                    dve.wait_ge(route_pe, 1)
                    tot = psum[5][:, 0:NQ * E].rearrange("p (q e) -> p q e", e=E)
                    r(dve.tensor_copy(cum[0][:], tot))
                    a = 0
                    for s in (1, 2, 4, 8, 16):
                        r(dve.tensor_copy(cum[1 - a][:, 0:s], cum[a][:, 0:s]))
                        r(dve.tensor_tensor(cum[1 - a][:, s:], cum[a][:, s:], cum[a][:, 0:NQ - s], ALU.add))
                        a = 1 - a
                    r(dve.tensor_scalar(count_i[:], cum[a][:, NQ - 1, :], float(P - 1), None, ALU.add))
                    r(dve.tensor_scalar(count_i[:], count_i[:], -P, None, ALU.bitwise_and))
                    r(dve.tensor_copy(padded[:], count_i[:]))
                    r(dve.memset(ends[:], 0.0))
                    for e in range(E):
                        r(dve.tensor_tensor(ends[:, e + 1:e + 2], ends[:, e:e + 1], padded[:, e:e + 1], ALU.add))
                    r(dve.tensor_tensor(row[:], cum[a][:], tot, ALU.subtract))
                    rank = psum[4][:, 0:NQ * E].rearrange("p (q e) -> p q e", e=E)
                    r(dve.tensor_tensor(row[:], row[:], rank, ALU.add))
                    r(dve.tensor_tensor(row[:], row[:], ends[:, 0:E].unsqueeze(1).to_broadcast(wide), ALU.add))
                    r(dve.tensor_tensor(row[:], row[:], onehot[:], ALU.mult))
                    r(dve.tensor_reduce(posf[:], row[:], AX_X, ALU.add))
                    dve.tensor_scalar(pos[:], posf[:], -1.0, None, ALU.add).then_inc(pos_done, 1)
                    dve.sem_inc(xn_inplace, 1)
                    r(dve.memset(tile_ef[:], 0.0))
                    for e in range(1, E):
                        r(dve.scalar_tensor_tensor(out=tile_ef[:], in0=tile_row[:], scalar=ends[0:1, e:e + 1],
                                                   in1=tile_ef[:], op0=ALU.is_ge, op1=ALU.add))
                    r(dve.tensor_copy(tile_e[:], tile_ef[:]))

                @block.scalar
                def _(act):
                    for b in range(B):
                        act.sem_inc(xnT_sb[b].sem, 1)
                        act.sem_inc(xnT_out[b], 16)
                    act.wait_ge(consts, 1)
                    act.activation(beta[:, 0, 0:1], halves[:, 0:1], ACT.Sigmoid)
                    with act.Fori(0, NCH) as i:
                        st = Step(act, i)
                        out16 = act.snap(16 * i + 16)
                        for b in range(B):
                            st.this(xnT_ps[b])
                            act.wait_ge(xnT_out[b], out16)
                            st.last(lg_ps[b])
                            act.copy(xnT_t[b][:].rearrange("p k n -> p (k n)"), psum[b][:, 0:KC * P]).then_inc(xnT_sb[b].sem, 1)
                    for b in range(B):
                        act.wait_ge(lg_sb[b].sem, NCH + 1)
                    act.activation(beta[:], logits[:, :, 0:H], ACT.Sigmoid).then_inc(beta_done, 1)
                    act.wait_ge(w_in, 16 * 6)
                    for k in range(KC):
                        act.activation(wo_sb[:, k, :], wo_sb[:, k, :], ACT.Copy, scale=nw_sb[:, 0:1]).then_inc(beta_done, 1)
                    act.wait_ge(beta_done, 1 + KC)

                @block.tensor
                def _(pe):
                    for b in range(B):
                        pe.sem_inc(lg_ps[b].sem, 1)
                    pe.wait_ge(consts, n_consts)
                    pe.wait_ge(w_in, 16 * 6)
                    with pe.Fori(0, NCH) as i:
                        st = Step(pe, i)
                        for b in range(B):
                            st.this(xn_done[b])
                            st.last(xnT_sb[b])
                            for k in range(KC):
                                ins = pe.transpose(psum[b][:, k * P:(k + 1) * P], xn_t[b][:, k, :], ident[:])
                            ins.then_inc(xnT_ps[b].sem, 1)
                        for b in range(B):
                            st.this(xnT_sb[b])
                            st.last(lg_sb[b])
                            for k in range(KC):
                                ins = pe.matmul(psum[2 + b][:, 0:H + E], xnT_t[b][:, k, :], wbr_sb[:, k, :],
                                                start=(k == 0), stop=(k == KC - 1))
                            ins.then_inc(lg_ps[b].sem, 1)
                    pe.wait_ge(onehot_done, 1)
                    oh = onehot16[:].rearrange("p q e -> p (q e)")
                    pe.matmul(psum[4][:, 0:NQ * E], up_incl16[:], oh, start=True, stop=True)
                    pe.matmul(psum[5][:, 0:NQ * E], ones16[:], oh, start=True, stop=True).then_inc(route_pe, 1)

        work = ExitStack()
        with work:
            def tmp(name, shape, dt=F32):
                return work.enter_context(nc.sbuf_tensor(name, shape, dt))

            xt = [tmp(f"xt{b}", [P, KC, P]) for b in range(B)]
            f32_t = tmp("f32_t", [P, NS, P])
            k16 = [tmp(f"k16_{z}", [P, NS, P], F16) for z in "hl"]
            kT16 = tmp("kT16", [P, B, 2, H, P], F16)
            qT16 = [tmp(f"qT16_{z}", [P, NS, P], F16) for z in "hl"]
            XT = [tmp(f"XT_{z}", [P, NS, P], F16) for z in "hl"]
            PT = [tmp(f"PT_{z}", [P, NS, P], F16) for z in "hl"]
            Pm = tmp("Pm", [P, NS, P // 2], F16)
            M = tmp("M", [P, NS, P], F16)
            Z = tmp("Z", [P, NS, P], F16)
            Fr = XT[1]
            Zf = [XT[0], M]
            v_sb = tmp("v_sb", [P, NS, DV])
            gate = tmp("gate", [P, NS, DV])
            S32 = tmp("S32", [P, NS, DV])
            S16 = [tmp(f"S16_{z}", [P, NS, DV], F16) for z in "hl"]
            ru32 = f32_t[:, 0:H, :].rearrange("p h (two n) -> p (h two) n", two=2)
            osq_sb = f32_t[:, H:, :].rearrange("p h (two n) -> p (h two) n", two=2)
            R16 = [tmp(f"R16_{z}", [P, NS, DV], F16) for z in "hl"]
            U16 = R16
            og = v_sb
            kss = tmp("kss", [P, NS])
            krn = tmp("krn", [P, NS])
            oss = tmp("oss", [P, NS])
            orn = tmp("orn", [P, NS])
            sq = f32_t

            g = lambda name: signal(name, 1)
            xt_in = [sem(f"xt_in{b}") for b in range(B)]
            VGp = [g(f"VGp{b}") for b in range(B)]
            Kp = [g(f"Kp{b}") for b in range(B)]
            Qp = [g(f"Qp{b}") for b in range(B)]
            ksq = [g(f"ksq{b}") for b in range(B)]
            kssum = [g(f"kssum{b}") for b in range(B)]
            krn1, krn_ok = g("krn1"), g("krn_ok")
            kn = [g(f"kn{b}") for b in range(B)]
            kh_ok = [g(f"kh_ok{b}") for b in range(B)]
            kl_ok = [g(f"kl_ok{b}") for b in range(B)]
            kTp = [g(f"kTp{b}") for b in range(B)]
            kT_ok = [g(f"kT_ok{b}") for b in range(B)]
            qh_ok = [g(f"qh_ok{b}") for b in range(B)]
            ql_ok = [g(f"ql_ok{b}") for b in range(B)]
            v_ok = [g(f"v_ok{b}") for b in range(B)]
            sig_ok = [g(f"sig_ok{b}") for b in range(B)]
            gate_ok = [g(f"gate_ok{b}") for b in range(B)]
            Gp = [g(f"Gp{b}") for b in range(B)]
            PTp = [g(f"PTp{b}") for b in range(B)]
            X32 = [g(f"X32_{b}") for b in range(B)]
            Xh_ok = [g(f"Xh_ok{b}") for b in range(B)]
            Xl_ok = [g(f"Xl_ok{b}") for b in range(B)]
            P32 = [g(f"P32_{b}") for b in range(B)]
            Ph_ok = [g(f"Ph_ok{b}") for b in range(B)]
            Pl_ok = [g(f"Pl_ok{b}") for b in range(B)]
            MZ0 = g("MZ0")
            Lp = sem("Lp")
            Lp_ok = sem("Lp_ok")
            dMp = sem("dMp")
            dZp = sem("dZp")
            dM_ok = sem("dM_ok")
            dZ_ok = sem("dZ_ok")
            Fp = [g(f"Fp{b}") for b in range(B)]
            F_ok = [g(f"F_ok{b}") for b in range(B)]
            Zp = [g(f"Zp{b}") for b in range(B)]
            Zh_ok = [g(f"Zh_ok{b}") for b in range(B)]
            Zl_ok = [g(f"Zl_ok{b}") for b in range(B)]
            KSp, R32, Rh_ok, Rl_ok = g("KSp"), g("R32"), g("Rh_ok"), g("Rl_ok")
            Up, U32s, Uh_ok, Ul_ok = g("Up"), g("U32s"), g("Uh_ok"), g("Ul_ok")
            Op, dSp = g("Op"), g("dSp")
            S32s, Sh_ok, Sl_ok = g("S32s"), g("Sh_ok"), g("Sl_ok")
            osq, oss_ok, orn1, orn_ok = g("osq"), g("oss_ok"), g("orn1"), g("orn_ok")
            og1, og_ok = g("og1"), g("og_ok")
            ogTp, ogT_ok, sp_, s_ok = g("ogTp"), g("ogT_ok"), g("sp_"), g("s_ok")
            s_out = sem("s_out")
            pm_zero = sem("pm_zero")

            ogT = tmp("ogT", [P, B, KC, P])
            s_sb = tmp("s_sb", [P, B, D])

            def h4(t, b):
                return t[:, H * b:H * (b + 1), :]

            def bank4(k):
                return psum[k][:].rearrange("p (h n) -> p h n", h=H)

            def bank8(k):
                return psum[k][:].rearrange("p (h n) -> p h n", h=NS)

            def evens(t, s, odd=0):
                return t.rearrange("p h (n two c) -> p h n two c", two=2, c=s)[:, :, :, odd, :]

            K_BANK, Q_BANK, VG_BANK = [0, 1], [2, 3], [4, 2]
            KT_BANK, G_BANK, PT_BANK = [0, 1], [3, 4], [2, 0]
            L_BANK, DM_BANK, DZ_BANK = 1, 3, 4
            F_BANK, Z_BANK = [2, 0], [3, 4]
            KS_BANK, U_BANK, O_BANK, DS_BANK, OGT_BANK, S_BANK = 1, 2, 0, 3, 4, 1

            with nc.Block() as block:
                @block.sync
                def _(sp):
                    sp.sem_inc(s_out, 16 * B)
                    with sp.Fori(0, NCH) as i:
                        st = Step(sp, i)
                        for b in range(B):
                            st.last(VGp[b])
                            sp.dma_start(xt[b][:].rearrange("p k n -> p (k n)"),
                                         xnT_d[bass.ds(2 * i + b, 1)].rearrange("a p n -> p (a n)")).then_inc(xt_in[b], 16)
                        st.this(s_ok)
                        for b in range(B):
                            sp.dma_start(s_d[bass.ds(2 * i + b, 1)].rearrange("a p n -> p (a n)"),
                                         s_sb[:, b, :]).then_inc(s_out, 16)
                    sp.wait_ge(s_out, 16 * B * (NCH + 1))

                @block.tensor
                def _(pe):
                    for s in (*VGp, *Kp, *Qp, *kTp, *Gp, *PTp, *Fp, *Zp, KSp, Up, Op, dSp, ogTp, sp_):
                        pe.sem_inc(s.sem, 1)

                    def pairs(outp, lhs, rhs, start=True, stop=True):
                        pe.matmul(outp, lhs[0], rhs[0], start=start, stop=False)
                        pe.matmul(outp, lhs[0], rhs[1], start=False, stop=False)
                        return pe.matmul(outp, lhs[1], rhs[0], start=False, stop=stop)

                    def attention(i):
                        st, lv = Step(pe, i), Levels(pe, i)
                        in16 = pe.snap(16 * i + 16)
                        for b in range(B):
                            pe.wait_ge(xt_in[b], in16)
                            st.last(*((osq, og1) if b == 0 else (s_ok,)))
                            for k in range(KC):
                                ins = pe.matmul(psum[K_BANK[b]][:], xt[b][:, k, :], wk_sb[:, k, :],
                                                start=(k == 0), stop=(k == KC - 1))
                            ins.then_inc(Kp[b].sem, 1)
                        for b in range(B):
                            st.last(U32s if b == 0 else S32s)
                            for h in range(H):
                                for k in range(KC):
                                    ins = pe.matmul(bank4(Q_BANK[b])[:, h, :], wq_sb[:, k, h * DK:(h + 1) * DK],
                                                    xt[b][:, k, :], start=(k == 0), stop=(k == KC - 1))
                            ins.then_inc(Qp[b].sem, 1)
                        for b in range(B):
                            if b == 0:
                                st.last(ogT_ok)
                            else:
                                st.this(qh_ok[0], ql_ok[0])
                            for k in range(KC):
                                ins = pe.matmul(psum[VG_BANK[b]][:], xt[b][:, k, :], wvg_sb[:, k, :],
                                                start=(k == 0), stop=(k == KC - 1))
                            ins.then_inc(VGp[b].sem, 1)
                        for b in range(B):
                            st.this(kn[b], kh_ok[b], kl_ok[b])
                            o16 = psum[KT_BANK[b]][:].bitcast(F16).rearrange("p (z h n) -> p z h n", z=2, h=H)
                            for z in range(2):
                                for h in range(H):
                                    ins = pe.transpose(o16[:, z, h, :], k16[z][:, H * b + h, :], ident16[:])
                            ins.then_inc(kTp[b].sem, 1)
                        for b in range(B):
                            st.this(kT_ok[b])
                            st.this(*((qh_ok[1], ql_ok[1]) if b == 0 else (v_ok[0], gate_ok[0])))
                            for h in range(H):
                                kT = [kT16[:, b, z, h, :] for z in range(2)]
                                ins = pairs(bank4(G_BANK[b])[:, h, :], kT, kT)
                            ins.then_inc(Gp[b].sem, 1)
                        for b in range(B):
                            st.this(*((v_ok[1], gate_ok[1]) if b == 0 else (kT_ok[0], qh_ok[1], ql_ok[1])))
                            for h in range(H):
                                kT = [kT16[:, b, z, h, :] for z in range(2)]
                                qT = [qT16[z][:, H * b + h, :] for z in range(2)]
                                ins = pairs(bank4(PT_BANK[b])[:, h, :], kT, qT)
                            ins.then_inc(PTp[b].sem, 1)
                        st.this(*Xh_ok, MZ0, kT_ok[1])
                        for l, s in enumerate(LEVELS):
                            if l:
                                lv.at(l - 1, Lp_ok, dM_ok, dZ_ok)
                            for h in range(NS):
                                ins = pe.matmul(bank8(L_BANK)[:, h, :].rearrange("p (n c) -> p n c", c=s),
                                                XT[0][:, h, :], evens(M[:, h:h + 1, :], s)[:, 0],
                                                start=True, stop=True)
                            ins.then_inc(Lp, 1)
                            lv.at(l, Lp_ok)
                            if l == 0:
                                st.this(*X32)
                            for h in range(NS):
                                ins = pe.matmul(bank8(DM_BANK)[:, h, :], Z[:, h, :], Pm[:, h, :], start=True, stop=True)
                            ins.then_inc(dMp, 1)
                            lv.at(l, dM_ok)
                            for h in range(NS):
                                ins = pe.matmul(bank8(DZ_BANK)[:, h, :].rearrange("p (n c) -> p n c", c=s),
                                                M[:, h, :], evens(ident16[:].unsqueeze(1), s, 1)[:, 0],
                                                start=True, stop=True)
                            ins.then_inc(dZp, 1)
                        lv.at(len(LEVELS) - 1, dM_ok, dZ_ok)
                        for b in range(B):
                            st.this(Xl_ok[b], P32[b])
                            for h in range(H * b, H * (b + 1)):
                                o = bank4(F_BANK[b])[:, h - H * b, :]
                                pe.matmul(o, ident16[:], ident16[:], start=True, stop=False)
                                pe.matmul(o, negid16[:], M[:, h, :], start=False, stop=False)
                                pe.matmul(o, XT[1][:, h, :], M[:, h, :], start=False, stop=False)
                                ins = pe.matmul(o, XT[0][:, h, :], M[:, h, :], start=False, stop=True)
                            ins.then_inc(Fp[b].sem, 1)
                        for b in range(B):
                            st.this(F_ok[b])
                            for h in range(H * b, H * (b + 1)):
                                o = bank4(Z_BANK[b])[:, h - H * b, :]
                                pe.matmul(o, ident16[:], Z[:, h, :], start=True, stop=False)
                                ins = pe.matmul(o, Fr[:, h, :], Z[:, h, :], start=False, stop=True)
                            ins.then_inc(Zp[b].sem, 1)
                        st.last(Sh_ok, Sl_ok)
                        for h in range(NS):
                            kT = [kT16[:, h // H, z, h % H, :] for z in range(2)]
                            ins = pairs(bank8(KS_BANK)[:, h, :], kT, [S16[z][:, h, :] for z in range(2)])
                        ins.then_inc(KSp.sem, 1)
                        st.this(*Zh_ok, *Zl_ok, Rh_ok, Rl_ok)
                        for h in range(NS):
                            ins = pairs(bank8(U_BANK)[:, h, :], [Zf[z][:, h, :] for z in range(2)],
                                        [R16[z][:, h, :] for z in range(2)])
                        ins.then_inc(Up.sem, 1)
                        st.this(*Ph_ok, *Pl_ok, Uh_ok, Ul_ok, F_ok[1])
                        for h in range(NS):
                            U = [U16[z][:, h, :] for z in range(2)]
                            pairs(bank8(O_BANK)[:, h, :], [qT16[z][:, h, :] for z in range(2)],
                                  [S16[z][:, h, :] for z in range(2)], stop=False)
                            ins = pairs(bank8(O_BANK)[:, h, :], [PT[z][:, h, :] for z in range(2)], U, start=False)
                        ins.then_inc(Op.sem, 1)
                        for h in range(NS):
                            ins = pairs(bank8(DS_BANK)[:, h, :], [k16[z][:, h, :] for z in range(2)],
                                        [U16[z][:, h, :] for z in range(2)])
                        ins.then_inc(dSp.sem, 1)
                        st.this(og_ok)
                        for b in range(B):
                            for k in range(KC):
                                ins = pe.transpose(psum[OGT_BANK][:, (b * KC + k) * P:(b * KC + k + 1) * P],
                                                   og[:, H * b + 2 * k:H * b + 2 * k + 2, :].rearrange("p h n -> p (h n)"),
                                                   ident[:])
                        ins.then_inc(ogTp.sem, 1)
                        st.this(ogT_ok, R32)
                        for b in range(B):
                            for k in range(KC):
                                ins = pe.matmul(psum[S_BANK][:, b * D:(b + 1) * D], ogT[:, b, k, :], wo_sb[:, k, :],
                                                start=(k == 0), stop=(k == KC - 1))
                        ins.then_inc(sp_.sem, 1)

                    with pe.Fori(0, NCH) as i:
                        attention(i)

                @block.vector
                def _(dve):
                    for s in (*kssum, *kn, *kh_ok, *ql_ok, *gate_ok, *X32, *Xh_ok, *P32, *Ph_ok, MZ0,
                              *Zl_ok, R32, Rh_ok, Rl_ok, U32s, Uh_ok, Ul_ok, S32s, Sh_ok,
                              Sl_ok, oss_ok, og1):
                        dve.sem_inc(s.sem, 1)
                    dve.memset(S32[:], 0.0).then_inc(pm_zero, 1)
                    for z in range(2):
                        dve.memset(S16[z][:], 0.0).then_inc(pm_zero, 1)
                    dve.wait_ge(pm_zero, 3)

                    def attention(i):
                        st, lv = Step(dve, i), Levels(dve, i)
                        for b in range(B):
                            st.this(ksq[b])
                            dve.tensor_reduce(kss[:, H * b:H * (b + 1)], h4(sq, b), AX_X, ALU.add).then_inc(kssum[b].sem, 1)
                        for b in range(B):
                            st.this(Qp[b], qh_ok[b])
                            st.last(Op)
                            dve.tensor_tensor(h4(qT16[1], b), bank4(Q_BANK[b]), h4(qT16[0], b), ALU.subtract).then_inc(ql_ok[b].sem, 1)
                        st.this(krn_ok)
                        for b in range(B):
                            st.this(kssum[b])
                            dve.tensor_tensor(h4(f32_t, b), bank4(K_BANK[b]),
                                              krn[:, H * b:H * (b + 1)].unsqueeze(2).to_broadcast([P, H, P]),
                                              ALU.mult).then_inc(kn[b].sem, 1)
                            st.this(kn[b])
                            st.last(dSp)
                            dve.tensor_copy(h4(k16[0], b), h4(f32_t, b)).then_inc(kh_ok[b].sem, 1)
                        for b in range(B):
                            st.this(sig_ok[b])
                            st.this(v_ok[b])
                            dve.tensor_tensor(h4(gate, b), psum[VG_BANK[b]][:, H * DV:].rearrange("p (h n) -> p h n", h=H),
                                              h4(gate, b), ALU.mult).then_inc(gate_ok[b].sem, 1)
                        st.last(Up)
                        dve.tensor_copy(M[:], pm1[:])
                        dve.tensor_copy(Z[:], pm1[:]).then_inc(MZ0.sem, 1)
                        bt = beta[:, bass.ds(2 * i, 2), :].rearrange("p b h -> p (b h)")
                        for b in range(B):
                            st.this(Gp[b], kl_ok[b], kh_ok[b])
                            for h in range(H):
                                ins = dve.scalar_tensor_tensor(out=f32_t[:, H * b + h, :], in0=bank4(G_BANK[b])[:, h, :],
                                                               scalar=bt[:, H * b + h:H * b + h + 1], in1=up_neg[:],
                                                               op0=ALU.mult, op1=ALU.mult)
                            ins.then_inc(X32[b].sem, 1)
                            st.this(X32[b])
                            st.last(Up)
                            dve.tensor_copy(h4(XT[0], b), h4(f32_t, b)).then_inc(Xh_ok[b].sem, 1)
                        for b in range(B):
                            st.this(PTp[b], Xl_ok[b], Xh_ok[b])
                            dve.tensor_tensor(h4(f32_t, b), bank4(PT_BANK[b]),
                                              up_incl[:].unsqueeze(1).to_broadcast([P, H, P]), ALU.mult).then_inc(P32[b].sem, 1)
                            st.this(P32[b])
                            st.last(Op)
                            dve.tensor_copy(h4(PT[0], b), h4(f32_t, b)).then_inc(Ph_ok[b].sem, 1)
                        for l, s in enumerate(LEVELS):
                            lv.at(l, Lp)
                            mask = lvl_mask[:, l, :].rearrange("p (n c) -> p n c", c=s).unsqueeze(1).to_broadcast([P, NS, P // 2 // s, s])
                            v = lambda k: bank8(k).rearrange("p h (n c) -> p h n c", c=s)
                            dve.tensor_tensor(Pm[:].rearrange("p h (n c) -> p h n c", c=s), v(L_BANK), mask, ALU.mult).then_inc(Lp_ok, 1)
                            lv.at(l, dMp)
                            if l == 0:
                                st.this(MZ0)
                            else:
                                lv.at(l - 1, dM_ok)
                            dve.tensor_tensor(evens(M[:], s), v(DM_BANK), evens(M[:], s), ALU.add).then_inc(dM_ok, 1)
                        for b in range(B):
                            st.this(Zh_ok[b])
                            st.last(Up)
                            dve.tensor_tensor(h4(Zf[1], b), bank4(Z_BANK[b]), h4(Zf[0], b), ALU.subtract).then_inc(Zl_ok[b].sem, 1)
                        st.this(KSp, *v_ok, *Pl_ok)
                        st.last(dSp)
                        dve.tensor_tensor(ru32, v_sb[:], bank8(KS_BANK), ALU.subtract).then_inc(R32.sem, 1)
                        st.this(R32)
                        dve.tensor_copy(R16[0][:], ru32).then_inc(Rh_ok.sem, 1)
                        st.this(Rh_ok)
                        dve.tensor_tensor(R16[1][:], ru32, R16[0][:], ALU.subtract).then_inc(Rl_ok.sem, 1)
                        st.this(Up, Rl_ok)
                        dve.tensor_tensor(ru32, bank8(U_BANK), bt.unsqueeze(2).to_broadcast([P, NS, DV]), ALU.mult).then_inc(U32s.sem, 1)
                        st.this(U32s)
                        dve.tensor_copy(U16[0][:], ru32).then_inc(Uh_ok.sem, 1)
                        st.this(Uh_ok)
                        dve.tensor_tensor(U16[1][:], ru32, U16[0][:], ALU.subtract).then_inc(Ul_ok.sem, 1)
                        st.this(dSp)
                        st.last(S32s, Sl_ok)
                        dve.tensor_tensor(S32[:], bank8(DS_BANK), S32[:], ALU.add).then_inc(S32s.sem, 1)
                        st.this(S32s)
                        dve.tensor_copy(S16[0][:], S32[:]).then_inc(Sh_ok.sem, 1)
                        st.this(Sh_ok)
                        dve.tensor_tensor(S16[1][:], S32[:], S16[0][:], ALU.subtract).then_inc(Sl_ok.sem, 1)
                        st.this(osq)
                        dve.tensor_reduce(oss[:], osq_sb, AX_X, ALU.add).then_inc(oss_ok.sem, 1)
                        st.this(Op, *gate_ok, R32)
                        dve.tensor_tensor(og[:], bank8(O_BANK), gate[:], ALU.mult).then_inc(og1.sem, 1)

                    with dve.Fori(0, NCH) as i:
                        attention(i)

                @block.scalar
                def _(act):
                    for s in (*ksq, *kT_ok, *qh_ok, *v_ok, *sig_ok, *F_ok, *Zh_ok, osq, ogT_ok, s_ok):
                        act.sem_inc(s.sem, 1)

                    def attention(i):
                        st, lv = Step(act, i), Levels(act, i)
                        for b in range(B):
                            st.this(Kp[b])
                            st.last(Ul_ok, oss_ok)
                            act.activation(h4(sq, b), bank4(K_BANK[b]), ACT.Square).then_inc(ksq[b].sem, 1)
                        for b in range(B):
                            st.this(Qp[b])
                            st.last(Op)
                            act.copy(h4(qT16[0], b), bank4(Q_BANK[b])).then_inc(qh_ok[b].sem, 1)
                        for b in range(B):
                            st.this(VGp[b])
                            st.last(ogTp, og1)
                            act.copy(h4(v_sb, b).rearrange("p h n -> p (h n)"), psum[VG_BANK[b]][:, 0:H * DV]).then_inc(v_ok[b].sem, 1)
                            act.activation(h4(gate, b).rearrange("p h n -> p (h n)"), psum[VG_BANK[b]][:, H * DV:],
                                           ACT.Sigmoid).then_inc(sig_ok[b].sem, 1)
                        for b in range(B):
                            st.this(kTp[b])
                            st.last(KSp)
                            act.copy(kT16[:, b].rearrange("p z h n -> p (z h n)"), psum[KT_BANK[b]][:].bitcast(F16)).then_inc(kT_ok[b].sem, 1)
                        for l, s in enumerate(LEVELS):
                            lv.at(l, dZp)
                            act.copy(evens(Z[:], s, 1), bank8(DZ_BANK).rearrange("p h (n c) -> p h n c", c=s)).then_inc(dZ_ok, 1)
                        for b in range(B):
                            st.this(Fp[b])
                            act.copy(h4(Fr, b), bank4(F_BANK[b])).then_inc(F_ok[b].sem, 1)
                        for b in range(B):
                            st.this(Zp[b])
                            st.last(Up)
                            act.copy(h4(Zf[0], b), bank4(Z_BANK[b])).then_inc(Zh_ok[b].sem, 1)
                        st.this(Op)
                        st.last(oss_ok)
                        act.activation(osq_sb, bank8(O_BANK), ACT.Square, scale=DV ** -0.5).then_inc(osq.sem, 1)
                        st.this(ogTp)
                        act.copy(ogT[:].rearrange("p b k n -> p (b k n)"), psum[OGT_BANK][:]).then_inc(ogT_ok.sem, 1)
                        st.this(sp_)
                        act.wait_ge(s_out, act.snap(16 * B * i + 16 * B))
                        act.copy(s_sb[:].rearrange("p b n -> p (b n)"), psum[S_BANK][:]).then_inc(s_ok.sem, 1)

                    with act.Fori(0, NCH) as i:
                        attention(i)

                @block.gpsimd
                def _(pool):
                    for s in (krn1, krn_ok, *kl_ok, *Xl_ok, *Pl_ok, orn1, orn_ok, og_ok):
                        pool.sem_inc(s.sem, 1)

                    def attention(i):
                        st = Step(pool, i)
                        st.this(*kssum)
                        pool.tensor_tensor(krn[:], kss[:], k_eps[:], ALU.add).then_inc(krn1.sem, 1)
                        st.this(krn1)
                        pool.tensor_tensor(krn[:], krn[:], halves[:, 0:NS], ALU.pow).then_inc(krn_ok.sem, 1)
                        for b in range(B):
                            st.this(kh_ok[b])
                            pool.tensor_tensor(h4(k16[1], b), h4(f32_t, b), h4(k16[0], b), ALU.subtract).then_inc(kl_ok[b].sem, 1)
                        for b in range(B):
                            st.this(Xh_ok[b])
                            st.last(Zp[b])
                            pool.tensor_tensor(h4(XT[1], b), h4(f32_t, b), h4(XT[0], b), ALU.subtract).then_inc(Xl_ok[b].sem, 1)
                        for b in range(B):
                            st.this(Ph_ok[b])
                            pool.tensor_tensor(h4(PT[1], b), h4(f32_t, b), h4(PT[0], b), ALU.subtract).then_inc(Pl_ok[b].sem, 1)
                        st.this(oss_ok)
                        pool.tensor_tensor(orn[:], oss[:], o_eps[:], ALU.add).then_inc(orn1.sem, 1)
                        st.this(orn1)
                        pool.tensor_tensor(orn[:], orn[:], halves[:, 0:NS], ALU.pow).then_inc(orn_ok.sem, 1)
                        st.this(orn_ok, og1)
                        pool.tensor_tensor(og[:], og[:], orn[:].unsqueeze(2).to_broadcast([P, NS, DV]), ALU.mult).then_inc(og_ok.sem, 1)

                    with pool.Fori(0, NCH) as i:
                        attention(i)

        work = ExitStack()
        with work:
            def tmp(name, shape, dt=F32):
                return work.enter_context(nc.sbuf_tensor(name, shape, dt))

            rows_in = sem("rows_in")
            xs = tmp("xs", [P, D])
            xsT = tmp("xsT", [P, KC, P])
            r_sb = tmp("r_sb", [P, HD])
            hT = tmp("hT", [P, HC, P])
            y_sb = tmp("y_sb", [P, D])
            xsTp, xsT_ok = signal("xsTp", 1), signal("xsT_ok", 1)
            hp = [signal(f"hp{k}", 1) for k in range(2)]
            relu_ok = [signal(f"relu_ok{k}", 1) for k in range(2)]
            rTp = [signal(f"rTp{k}", 1) for k in range(2)]
            sq_ok = [signal(f"sq_ok{k}", 1) for k in range(2)]
            yp, y_ok = signal("yp", 1), signal("y_ok", 1)
            y_out = sem("y_out")
            XS_BANK, H_BANK, Y_BANK = 5, [6, 7], 4

            with nc.Block() as block:
                @block.sync
                def _(sp):
                    sp.sem_inc(y_out, 16)
                    with sp.Fori(0, NT) as j:
                        st = Step(sp, j)
                        st.last(xsTp)
                        sp.dma_start(xs[:], sorted_x_d.rearrange("(j p) d -> j p d", p=P)[bass.ds(j, 1)].rearrange("a p n -> p (a n)")).then_inc(rows_in, 16)
                        st.this(y_ok)
                        sp.dma_start(sorted_y_d.rearrange("(j p) d -> j p d", p=P)[bass.ds(j, 1)].rearrange("a p n -> p (a n)"), y_sb[:]).then_inc(y_out, 16)
                    sp.wait_ge(y_out, 16 * (NT + 1))

                @block.tensor
                def _(pe):
                    for s in (xsTp, *hp, *rTp, yp):
                        pe.sem_inc(s.sem, 1)

                    def expert_tile(j):
                        st = Step(pe, j)
                        ex = pe.value_load(tile_e[0:1, bass.ds(j, 1)], min_val=0, max_val=E - 1)
                        pe.wait_ge(rows_in, pe.snap(16 * j + 16))
                        st.last(xsT_ok)
                        for k in range(KC):
                            ins = pe.transpose(psum[XS_BANK][:, k * P:(k + 1) * P], xs[:, k * P:(k + 1) * P], ident[:])
                        ins.then_inc(xsTp.sem, 1)
                        st.this(xsT_ok)
                        for n in range(2):
                            st.last(sq_ok[n])
                            for k in range(KC):
                                ins = pe.matmul(psum[H_BANK[n]][:], xsT[:, k, :],
                                                fc_sb[:, bass.ds(ex, 1), k, n * 512:(n + 1) * 512].rearrange("p a n -> p (a n)"),
                                                start=(k == 0), stop=(k == KC - 1))
                            ins.then_inc(hp[n].sem, 1)
                        for n in range(2):
                            st.this(relu_ok[n])
                            for c in range(4):
                                ins = pe.transpose(psum[H_BANK[n]][:, c * P:(c + 1) * P],
                                                   r_sb[:, n * 512 + c * P:n * 512 + (c + 1) * P], ident[:])
                            ins.then_inc(rTp[n].sem, 1)
                        st.last(y_ok)
                        for c in range(HC):
                            if c % 4 == 0:
                                st.this(sq_ok[c // 4])
                            ins = pe.matmul(psum[Y_BANK][:, 0:D], hT[:, c, :],
                                            pj_sb[:, bass.ds(ex, 1), c, :].rearrange("p a n -> p (a n)"),
                                            start=(c == 0), stop=(c == HC - 1))
                        ins.then_inc(yp.sem, 1)

                    with pe.Fori(0, NT) as j:
                        expert_tile(j)

                @block.scalar
                def _(act):
                    for s in (xsT_ok, *relu_ok, *sq_ok, y_ok):
                        act.sem_inc(s.sem, 1)

                    def expert_tile(j):
                        st = Step(act, j)
                        st.this(xsTp)
                        st.last(*hp)
                        act.copy(xsT[:].rearrange("p k n -> p (k n)"), psum[XS_BANK][:, 0:KC * P]).then_inc(xsT_ok.sem, 1)
                        for n in range(2):
                            st.this(hp[n])
                            st.last(rTp[n])
                            act.activation(r_sb[:, n * 512:(n + 1) * 512], psum[H_BANK[n]][:], ACT.Relu).then_inc(relu_ok[n].sem, 1)
                        for n in range(2):
                            st.this(rTp[n])
                            st.last(yp)
                            act.activation(hT[:, 4 * n:4 * n + 4, :].rearrange("p c n -> p (c n)"), psum[H_BANK[n]][:],
                                           ACT.Square).then_inc(sq_ok[n].sem, 1)
                        st.this(yp)
                        act.wait_ge(y_out, act.snap(16 * j + 16))
                        act.copy(y_sb[:], psum[Y_BANK][:, 0:D]).then_inc(y_ok.sem, 1)

                    with act.Fori(0, NT) as j:
                        expert_tile(j)

            xf = tmp("xf", [P, B, D])
            sf = tmp("sf", [P, B, D])
            yf = tmp("yf", [P, B, D])
            gf = tmp("gf", [P, B, D])
            xs_in, gathered = sem("xs_in"), sem("gathered")
            sgm, f1, f2, f3 = signal("sgm", 1), signal("f1", 1), signal("f2", 1), signal("f3", 1)
            o_out = sem("o_out")
            x_v = x.rearrange("b (c p) d -> c p b d", p=P)
            o_v = out.rearrange("b (c p) d -> c p b d", p=P)
            with nc.Block() as block:
                @block.sync
                def _(sp):
                    with sp.Fori(0, NCH) as i:
                        st = Step(sp, i)
                        st.last(f3)
                        sp.dma_start(xf[:], x_v[bass.ds(i, 1)].rearrange("a p b d -> p (a b) d")).then_inc(xs_in, 16)
                        sp.dma_start(sf[:], s_d[bass.ds(2 * i, 2)].rearrange("b p d -> p b d")).then_inc(xs_in, 16)

                @block.gpsimd
                def _(pool):
                    for i in range(NCH):
                        pool.wait_ge(f1.sem, i + 1)
                        for b in range(B):
                            q = 2 * i + b
                            pool.indirect_dma_start(
                                out=yf[:, b, :], out_offset=None, in_=sorted_y_d,
                                in_offset=bass.IndirectOffsetOnAxis(ap=pos[:, q:q + 1].bitcast(U32), axis=0),
                            ).then_inc(gathered, 16)

                @block.scalar
                def _(act):
                    act.sem_inc(sgm.sem, 1)
                    with act.Fori(0, NCH) as i:
                        st = Step(act, i)
                        act.wait_ge(gathered, act.snap(32 * i + 32))
                        st.last(f1)
                        act.activation(gf[:], yf[:], ACT.Sigmoid).then_inc(sgm.sem, 1)
                        st.this(f3)
                        act.dma_start(o_v[bass.ds(i, 1)].rearrange("a p b d -> p (a b) d"), gf[:]).then_inc(o_out, 16)
                        act.wait_ge(o_out, act.snap(16 * i + 16))
                    act.wait_ge(o_out, 16 * NCH)

                @block.vector
                def _(dve):
                    for s in (f1, f2, f3):
                        dve.sem_inc(s.sem, 1)
                    with dve.Fori(0, NCH) as i:
                        st = Step(dve, i)
                        st.this(sgm)
                        dve.wait_ge(gathered, dve.snap(32 * i + 32))
                        dve.tensor_tensor(gf[:], gf[:], yf[:], ALU.mult).then_inc(f1.sem, 1)
                        st.this(f1)
                        dve.wait_ge(xs_in, dve.snap(32 * i + 32))
                        dve.tensor_tensor(gf[:], gf[:], sf[:], ALU.mult).then_inc(f2.sem, 1)
                        st.this(f2)
                        dve.tensor_tensor(gf[:], gf[:], xf[:], ALU.add).then_inc(f3.sem, 1)


def kernel(L0_attn_x, L0_attn_Wq, L0_attn_Wk, L0_attn_Wv, L0_attn_Wb, L0_attn_Wg, L0_attn_Wo,
           L0_attn_norm_w, L0_ffn_router_w, L0_ffn_expert_fc, L0_ffn_expert_proj):
    import numpy as np
    import concourse.bacc as bacc
    from concourse.bass_utils import run_bass_kernel_spmd

    as_np = lambda a: np.asarray(a)
    arrays = {
        "x": as_np(L0_attn_x),
        "wq": as_np(L0_attn_Wq),
        "wk": as_np(L0_attn_Wk),
        "wvg": np.concatenate([as_np(L0_attn_Wv), as_np(L0_attn_Wg)], axis=1),
        "wbr": np.concatenate([as_np(L0_attn_Wb), as_np(L0_ffn_router_w).T], axis=1),
        "wo": as_np(L0_attn_Wo),
        "norm_w": np.tile(as_np(L0_attn_norm_w), P // DV).reshape(P, 1),
        "fc": as_np(L0_ffn_expert_fc),
        "pj": np.transpose(as_np(L0_ffn_expert_proj), (0, 2, 1)),
    }
    arrays = {f"in_{n}": np.ascontiguousarray(a) for n, a in arrays.items()}
    nc = bacc.Bacc("TRN2", target_bir_lowering=False, num_devices=1)
    args = [nc.dram_tensor(n, a.shape, mybir.dt.from_np(a.dtype), kind="ExternalInput").ap()
            for n, a in arrays.items()]
    out = nc.dram_tensor("out_x", [B, N, D], F32, kind="ExternalOutput").ap()
    build_program(nc, *args, out)
    result = run_bass_kernel_spmd(nc, [arrays], core_ids=[0])
    return result.results[0]["out_x"]
```
